# Optimizing a Trainium2 kernel written in Bass

```python
import numpy as np
import jax
import jax.numpy as jnp

def _softmax(x, axis=-1):
    return jax.nn.softmax(x, axis=axis)

def _gelu(x):
    return jax.nn.gelu(x, approximate=True)

def _silu(x):
    return jax.nn.silu(x)

def _sigmoid(x):
    return jax.nn.sigmoid(x)

def _layernorm(x, axis=-1, eps=1e-05):
    m = jnp.mean(x, axis=axis, keepdims=True)
    v = jnp.var(x, axis=axis, keepdims=True)
    return (x - m) / jnp.sqrt(v + eps)

def _scatter_add(tgt, idx, src, axis=0):
    return tgt.at[idx].add(src)

def _segment_sum(src, seg, n):
    return jax.ops.segment_sum(src, seg, n)
kernel_name = 'mk_adj_preln_d1_adj_r2_415518'

def setup_inputs(seed: int=0):
    np.random.seed(seed)
    _w = jnp.asarray

    def _rec_inputs():
        import jax
        import jax.numpy as jnp
        _gk = jax.random.key(seed)
        x = -0.0005207 + 1.001 * jax.random.normal(jax.random.fold_in(_gk, 1), (8192, 256), jnp.float32)
        _a = jax.random.bernoulli(jax.random.fold_in(_gk, 2), 0.000976562, (8192, 8192))
        _a = jnp.logical_or(_a, jnp.eye(8192, dtype=bool))
        _af = _a.astype(jnp.float32)
        _af = _af * jax.random.uniform(jax.random.fold_in(_gk, 3), (8192, 8192), jnp.float32, 0.05, 1)
        adj = _af
        return (x, adj)
    x, adj = _rec_inputs()

    def _L0_gnn_setup():
        import jax, jax.numpy as jnp
        import numpy as np
        N = 2048
        IN_F = 256
        OUT_F = 256
        key = jax.random.key(seed)
        k1, k2, k3, k4 = jax.random.split(key, 4)
        x = jax.random.normal(k1, (N, IN_F), dtype=jnp.float32)
        adj = jax.random.uniform(k2, (N, N), dtype=jnp.float32)
        bound = 1.0 / np.sqrt(IN_F)
        W = jax.random.uniform(k3, (OUT_F, IN_F), minval=-bound, maxval=bound, dtype=jnp.float32)
        b = jax.random.uniform(k4, (OUT_F,), minval=-bound, maxval=bound, dtype=jnp.float32)
        return {'x': x, 'adj': adj, 'W': W, 'b': b}
    _L0_gnn_all = _L0_gnn_setup()
    _L0_gnn_in = {k: v for k, v in _L0_gnn_all.items() if k in ('W', 'b')}
    del _L0_gnn_all
    return {'x': x, 'adj': adj, 'L0_gnn_W': _L0_gnn_in['W'], 'L0_gnn_b': _L0_gnn_in['b']}

def reference(x, adj, L0_gnn_W, L0_gnn_b):
    import jax
    import jax.numpy as jnp

    def _L0_gnn_ref(x, adj, W, b):
        import jax, jax.numpy as jnp
        import numpy as np
        N = 2048
        IN_F = 256
        OUT_F = 256
        adj_hat = adj + jnp.eye(adj.shape[0], dtype=adj.dtype)
        d = 1.0 / jnp.sqrt(adj_hat.sum(axis=1))
        norm_adj = d[:, None] * adj_hat * d[None, :]
        h = norm_adj @ x
        return h @ W.T + b
    h = jnp.maximum(_layernorm(x, axis=-1), 0.0)
    x = x + _L0_gnn_ref(h, adj, L0_gnn_W, L0_gnn_b)
    return x

_drawn_inputs = setup_inputs


def setup_inputs(seed=0):
    import zlib

    import numpy as np

    out = dict(_drawn_inputs(seed))
    spreads = {}
    factors = {}
    for name, (base, spread) in spreads.items():
        noise = np.random.default_rng([zlib.crc32(name.encode()), seed]).standard_normal(out[name].shape)
        drawn = base * np.exp(spread * noise) if base else spread * noise
        out[name] = jnp.asarray(drawn.astype(out[name].dtype))
    for name, factor in factors.items():
        out[name] = (out[name] * factor).astype(out[name].dtype)
    return out
```

```python
from contextlib import ExitStack

import concourse.bass as bass
from concourse import mybir


P = 128
N = 8192
F = 256
R = 512
C = R // P
BLOCKS = N // R
GROUP = 4
GROUPS = BLOCKS // GROUP
BODY = 4
AHEAD = C * BODY
ROW_BODIES = BLOCKS // BODY
LN_EPS = 1e-5
GW = 2 * F + 2
SUMMED = F + 2

SUM4, MIX4, MUL4 = "NNNN", "TNTN", "TTTT"
PASS1_LOOPS = [[(SUM4, 2), (SUM4, 2)], [(MIX4, 2), (SUM4, 2)], [(MIX4, 2), (MIX4, 2)], [(MIX4, 2), (MUL4, 2)]]


class Phase:

    def __init__(self, second, group, loops, bodies_before, t_before, rows_before, acc_before):
        self.second, self.group, self.loops = second, group, loops
        self.row0 = GROUP * group
        self.bodies = sum(n for _, n in loops)
        self.t_units = sum(kind.count("T") * n for kind, n in loops)
        self.n_units = sum(kind.count("N") * n for kind, n in loops)
        self.t_first = GROUP * group if second else 0
        self.n_first = GROUP * group
        self.bodies_before, self.t_before = bodies_before, t_before
        self.rows_before, self.acc_before = rows_before, acc_before

    def parts(self):
        body = t = n = 0
        for kind, count in self.loops:
            yield kind, count, body, t, n
            body += count
            t += count * kind.count("T")
            n += count * kind.count("N")


def phases():
    found, bodies, t, rows, acc = [], 0, 0, 0, 0
    plans = [(False, g, PASS1_LOOPS[g]) for g in range(GROUPS)]
    plans += [(True, g, [(MUL4, GROUPS - g)]) for g in range(GROUPS)]
    for second, g, loops in plans:
        ph = Phase(second, g, loops, bodies, t, rows, acc)
        found.append(ph)
        bodies += GROUP * ph.bodies
        t += GROUP * ph.t_units
        rows += GROUP
        acc += GROUP if ph.t_units else 0
    return found


def gnn_kernel(nc, x_rows, adj_t, adj_n, w_t, bias, out_rows):
    f32, f32r = mybir.dt.float32, mybir.dt.float32r
    ALU, ACT, AX = mybir.AluOpType, mybir.ActivationFunctionType, mybir.AxisListType.X
    PHASES = phases()
    FIRST, SECOND = PHASES[:GROUPS], PHASES[GROUPS:]
    base_dram = nc.dram_tensor("base_dram", (BLOCKS, P, C, F), f32)

    ctx = ExitStack()
    with ctx:
        def sb(name, shape, dt=f32):
            return ctx.enter_context(nc.sbuf_tensor(name, shape, dt))

        def pb(name, shape):
            return ctx.enter_context(nc.psum_tensor(name, shape, f32))

        def sem(name):
            return ctx.enter_context(nc.semaphore(name))

        G = sb("G", [P, N // P, GW], f32r)
        raw = [sb(f"raw{s}", [P, C, R]) for s in range(BODY)]
        a_hi = sb("a_hi", [P, C, R], f32r)
        a_lo = sb("a_lo", [P, C, R], f32r)
        wt = sb("wt", [P, 2, F])
        bias_all = sb("bias_all", [P, F])
        ident = sb("ident", [P, P])
        zeros = sb("zeros", [P, P], f32r)
        minus_half = sb("minus_half", [P, C])
        x_in = sb("x_in", [P, C, F])
        x_bias = sb("x_bias", [P, C, F])
        h = sb("h", [P, C, F])
        h_t = sb("h_t", [P, 2, R])
        stats = sb("stats", [P, C, 6])
        meanvar = sb("meanvar", [P, C, 2])
        var_eps = sb("var_eps", [P, C])
        rstd = sb("rstd", [P, C])
        newton = sb("newton", [P, C])
        sums = sb("sums", [P, C, BLOCKS])
        total = sb("total", [P, C])
        total2 = sb("total2", [P, C])
        d_all = sb("d_all", [P, N // P])
        part = sb("part", [P, C, SUMMED])
        g_all = sb("g_all", [P, C, F])
        base_in = x_in
        scaled = h
        result = g_all

        acc = pb("acc", [P, C, 512])
        tr_ps = pb("tr_ps", [P, 2, 512])
        g_ps = pb("g_ps", [P, 2, 512])

        raw_in = [sem(f"raw_in{s}") for s in range(BODY)]
        act_done = sem("act_done")
        dve_done = sem("dve_done")
        tile_used = sem("tile_used")
        const_in = sem("const_in")
        ident0 = sem("ident0")
        const_ready = sem("const_ready")
        x_here = sem("x_here")
        x_free = sem("x_free")
        stats_ready = sem("stats_ready")
        pool_step = sem("pool_step")
        h_ready = sem("h_ready")
        tr_ready = sem("tr_ready")
        ht_ready = sem("ht_ready")
        g_ready = sem("g_ready")
        g_used = sem("g_used")
        act_sums = sem("act_sums")
        sums_free = sem("sums_free")
        total_ready = sem("total_ready")
        d_ready = sem("d_ready")
        dve_step = sem("dve_step")
        G_ready = sem("G_ready")
        base_ready = sem("base_ready")
        base_stored = sem("base_stored")
        base_here = sem("base_here")
        acc_free = sem("acc_free")
        scaled_ready = sem("scaled_ready")
        out_ready = sem("out_ready")
        out_stored = sem("out_stored")

        pool_gate = sem("pool_gate")
        dve_gate = sem("dve_gate")

        def gate(eng, signal):
            eng.sem_inc(signal, 1)

        block = ctx.enter_context(nc.Block())

        @block.sync
        def _(sp):
            sp.dma_start(wt[:, :, :], w_t).then_inc(const_in, 16)
            sp.dma_start(bias_all[:, :], bias[0:1, :].broadcast_to([P, F])).then_inc(const_in, 16)

            def load(ph, row, kind, body, t0, n0, i):
                t, n = t0 + i * kind.count("T"), n0 + i * kind.count("N")
                for s, what in enumerate(kind):
                    unit = BODY * body + s
                    sp.wait_ge(act_done, C * unit + C)
                    sp.wait_ge(dve_done, C * unit + C)
                    if what == "T":
                        src = adj_t[bass.ds(ph.row0 + row, 1), bass.ds(ph.t_first + t, 1), :, :, :]
                        t = t + 1
                    else:
                        src = adj_n[bass.ds(ph.row0 + row, 1), bass.ds(ph.n_first + n, 1), :, :, :]
                        n = n + 1
                    sp.dma_start(raw[s][:, :, :], src.rearrange("a b p c j -> (a b p) c j")).then_inc(raw_in[s], 16)

            for ph in PHASES:
                with sp.Fori(0, GROUP) as row:
                    if not ph.second:
                        sp.wait_ge(x_free, ph.rows_before + row + 1)
                        sp.dma_start(x_in[:, :, :], x_rows[bass.ds(ph.row0 + row, 1), :, :, :].rearrange(
                            "a p c f -> (a p) c f")).then_inc(x_here, 16)
                    for kind, count, body0, t0, n0 in ph.parts():
                        with sp.Fori(0, count) as i:
                            load(ph, row, kind, ph.bodies_before + ph.bodies * row + body0 + i, t0, n0, i)

        @block.gpsimd
        def _(pool):
            pool.memset(ident[:, :], 0.0).then_inc(ident0, 1)
            pool.memset(minus_half[:, :], -0.5)
            pool.memset(zeros[:, :].bitcast(f32), 0.0)
            pool.memset(G[:, :, F:F + 2].bitcast(f32), 1.0)
            pool.wait_ge(ident0, 1)
            pool.affine_select(out=ident[:, :], in_=ident[:, :], compare_op=ALU.not_equal, fill=1.0, base=0,
                               pattern=[[-1, P]], channel_multiplier=1).then_inc(const_ready, 1)
            pool.wait_ge(const_ready, 1)
            pool.wait_ge(const_in, 32)
            STEPS = 10

            def rsqrt(step, out, v):
                step(pool.tensor_tensor(out, v, minus_half[:, :], ALU.pow))
                step(pool.tensor_tensor(newton[:, :], out, out, ALU.mult))
                step(pool.tensor_tensor(newton[:, :], newton[:, :], v, ALU.mult))
                step(pool.tensor_scalar(newton[:, :], newton[:, :], -0.5, 1.5, ALU.mult, ALU.add))
                return pool.tensor_tensor(out, out, newton[:, :], ALU.mult)

            for ph in FIRST:
                with pool.Fori(0, GROUP) as row:
                    done = [0]
                    at = ph.rows_before + row

                    def step(ins):
                        done[0] += 1
                        ins.then_inc(pool_step, 1)
                        pool.wait_ge(pool_step, at * STEPS + done[0])
                        gate(pool, pool_gate)

                    pool.wait_ge(stats_ready, at + 1)
                    gate(pool, pool_gate)
                    step(pool.tensor_scalar(var_eps[:, :], meanvar[:, :, 1], LN_EPS, None, ALU.add))
                    step(rsqrt(step, rstd[:, :], var_eps[:, :]))
                    for c in range(C):
                        last = pool.tensor_scalar(h[:, c, :], x_in[:, c, :], meanvar[:, c, 0:1], rstd[:, c:c + 1],
                                                  ALU.subtract, ALU.mult)
                    last.then_inc(h_ready, 1)
                    bias_c = bias_all[:, :].rearrange("p (a f) -> p a f", a=1).broadcast_to([P, C, F])
                    pool.tensor_tensor(x_bias[:, :, :], x_in[:, :, :], bias_c, ALU.add).then_inc(x_free, 1)
                    pool.wait_ge(total_ready, at + 1)
                    rsqrt(step, total2[:, :], total[:, :]).then_inc(d_ready, 1)
                    assert done[0] == STEPS
                    pool.wait_ge(base_ready, at + 1)
                    gate(pool, pool_gate)
                    pool.dma_start(base_dram[bass.ds(at, 1), :, :, :].rearrange("a p c f -> (a p) c f"),
                                   x_bias[:, :, :]).then_inc(base_stored, 16)
                    pool.wait_ge(base_stored, 16 * at + 16)
            for ph in SECOND:
                with pool.Fori(0, GROUP) as row:
                    at = ph.row0 + row
                    pool.wait_ge(out_ready, at + 1)
                    gate(pool, pool_gate)
                    pool.dma_start(base_in[:, :, :], base_dram[bass.ds(at, 1), :, :, :].rearrange(
                        "a p c f -> (a p) c f")).then_inc(base_here, 16)
                    pool.wait_ge(out_ready, at + 2)
                    gate(pool, pool_gate)
                    pool.dma_start(out_rows[bass.ds(at, 1), :, :, :].rearrange("a p c f -> (a p) c f"),
                                   result[:, :, :]).then_inc(out_stored, 16)
                    pool.wait_ge(out_stored, 16 * at + 16)

        @block.scalar
        def _(act):
            act.sem_inc(act_done, AHEAD)

            def units(ph, row, kind, body, t0, n0, i):
                t = ph.t_before + ph.t_units * row + t0 + i * kind.count("T")
                n = n0 + i * kind.count("N")
                for s, what in enumerate(kind):
                    act.wait_ge(raw_in[s], 16 * (body + 1))
                    if what == "T":
                        for b in range(C):
                            act.wait_ge(tile_used, C * t + b + 1)
                            nc.scalar.copy(a_hi[:, b, :], raw[s][:, b, :]).then_inc(act_done, 1)
                        t = t + 1
                    else:
                        for c in range(C // 2):
                            nc.scalar.activation(raw[s][:, c, :], raw[s][:, c, :], ACT.Copy,
                                                 accum_out=sums[:, c, bass.ds(n, 1)]).then_inc(act_done, 2)
                        n = n + 1

            for ph in FIRST:
                with act.Fori(0, GROUP) as row:
                    at = ph.rows_before + row
                    for k, (kind, count, body0, t0, n0) in enumerate(ph.parts()):
                        if n0 == 0 and "N" in kind:
                            act.wait_ge(sums_free, at + 1)
                        with act.Fori(0, count) as i:
                            units(ph, row, kind, ph.bodies_before + ph.bodies * row + body0 + i, t0, n0, i)
                        if k == 0:
                            act.wait_ge(tr_ready, at + 1)
                            nc.scalar.activation(h_t[:, 0, :], tr_ps[:, 0, :], ACT.Relu)
                            nc.scalar.activation(h_t[:, 1, :], tr_ps[:, 1, :], ACT.Relu).then_inc(ht_ready, 1)
            for ph in SECOND:
                with act.Fori(0, GROUP) as row:
                    at = ph.row0 + row
                    for kind, count, body0, t0, n0 in ph.parts():
                        with act.Fori(0, count) as i:
                            units(ph, row, kind, ph.bodies_before + ph.bodies * row + body0 + i, t0, n0, i)
                    act.wait_ge(tile_used, C * (ph.t_before + ph.t_units * (row + 1)) + C)
                    act.wait_ge(out_ready, at + 1)
                    for c in range(C):
                        nc.scalar.activation(scaled[:, c, :], acc[:, c, F:2 * F], ACT.Copy,
                                             scale=d_all[:, bass.ds(C * at + c, 1)]).then_inc(scaled_ready, 1)

        @block.vector
        def _(dve):
            dve.sem_inc(dve_done, AHEAD)
            dve.sem_inc(acc_free, C)
            for buffer_free in (x_free, g_used, sums_free, out_ready):
                dve.sem_inc(buffer_free, 1)

            def steps(ph):
                return 3 if ph.t_units else 2

            def steps_before(ph):
                return GROUP * sum(steps(p) for p in FIRST[:ph.group])

            def units(ph, row, kind, body, t0, n0, i):
                n = n0 + i * kind.count("N")
                for s, what in enumerate(kind):
                    if what == "T":
                        for b in range(C):
                            dve.wait_ge(act_done, AHEAD + C * (BODY * body + s) + b + 1)
                            nc.vector.tensor_tensor(a_lo[:, b, :], raw[s][:, b, :], a_hi[:, b, :].bitcast(f32),
                                                    ALU.subtract).then_inc(dve_done, 1)
                    else:
                        dve.wait_ge(raw_in[s], 16 * (body + 1))
                        nc.vector.tensor_reduce(sums[:, C // 2:C, bass.ds(n, 1)], raw[s][:, C // 2:C, :], AX,
                                                ALU.add).then_inc(dve_done, C)
                        n = n + 1

            for ph in FIRST:
                with dve.Fori(0, GROUP) as row:
                    done = [0]
                    at = ph.rows_before + row

                    def step(ins):
                        done[0] += 1
                        ins.then_inc(dve_step, 1)
                        dve.wait_ge(dve_step, steps_before(ph) + row * steps(ph) + done[0])

                    dve.wait_ge(x_here, 16 * at + 16)
                    for c in range(C):
                        last = nc.vector.bn_stats(stats[:, c, :], x_in[:, c, :])
                    step(last)
                    gate(dve, dve_gate)
                    for c in range(C):
                        last = nc.vector.bn_aggr(meanvar[:, c, :], stats[:, c, :])
                    last.then_inc(stats_ready, 1)
                    for kind, count, body0, t0, n0 in ph.parts():
                        with dve.Fori(0, count) as i:
                            units(ph, row, kind, ph.bodies_before + ph.bodies * row + body0 + i, t0, n0, i)
                    row_done = AHEAD + C * BODY * (ph.bodies_before + ph.bodies * (row + 1))
                    dve.wait_ge(act_done, row_done)
                    dve.wait_ge(dve_done, row_done)
                    nc.vector.tensor_reduce(total[:, :], sums[:, :, 0:ph.n_units], AX, ALU.add).then_inc(sums_free, 1)
                    dve.wait_ge(sums_free, at + 2)
                    if ph.t_units:
                        dve.wait_ge(tile_used, C * (ph.t_before + ph.t_units * (row + 1)) + C)
                        for c in range(C):
                            nc.vector.tensor_copy(part[:, c, :], acc[:, c, 0:SUMMED]).then_inc(acc_free, 1)
                        dve.wait_ge(acc_free, C * (ph.acc_before + row + 2))
                        nc.vector.scalar_tensor_tensor(out=total[:, :], in0=part[:, :, F], scalar=1.0,
                                                       in1=total[:, :], op0=ALU.add, op1=ALU.add).then_inc(total_ready, 1)
                    else:
                        nc.vector.tensor_scalar(total[:, :], total[:, :], 1.0, None, ALU.add).then_inc(total_ready, 1)
                    dve.wait_ge(d_ready, at + 1)
                    step(nc.vector.tensor_copy(d_all[:, bass.ds(C * at, C)], total2[:, :]))
                    dve.wait_ge(g_ready, at + 1)
                    for c in range(C):
                        g_c = g_ps[:, c // 2, F * (c % 2):F * (c % 2) + F]
                        nc.vector.tensor_scalar(g_all[:, c, :], g_c, total2[:, c:c + 1], None, ALU.mult)
                        last = nc.vector.tensor_scalar(G[:, bass.ds(C * at + c, 1), 0:F], g_c, total2[:, c:c + 1], None, ALU.mult)
                    last.then_inc(g_used, 1)
                    dve.wait_ge(g_used, at + 2)
                    nc.vector.tensor_tensor(G[:, bass.ds(C * at, C), F + 2:GW], g_all[:, :, :],
                                            G[:, bass.ds(C * at, C), 0:F].bitcast(f32), ALU.subtract).then_inc(G_ready, 1)
                    if ph.t_units:
                        step(nc.vector.tensor_tensor(g_all[:, :, :], g_all[:, :, :], part[:, :, 0:F], ALU.add))
                    dve.wait_ge(x_free, at + 2)
                    for c in range(C):
                        last = nc.vector.scalar_tensor_tensor(out=x_bias[:, c, :], in0=g_all[:, c, :],
                                                              scalar=total2[:, c:c + 1], in1=x_bias[:, c, :],
                                                              op0=ALU.mult, op1=ALU.add)
                    last.then_inc(base_ready, 1)
                    assert done[0] == steps(ph)
            for ph in SECOND:
                with dve.Fori(0, GROUP) as row:
                    at = ph.row0 + row
                    for kind, count, body0, t0, n0 in ph.parts():
                        with dve.Fori(0, count) as i:
                            units(ph, row, kind, ph.bodies_before + ph.bodies * row + body0 + i, t0, n0, i)
                    dve.wait_ge(base_here, 16 * at + 16)
                    for c in range(C):
                        dve.wait_ge(scaled_ready, C * at + c + 1)
                        nc.vector.scalar_tensor_tensor(out=scaled[:, c, :], in0=acc[:, c, 0:F],
                                                       scalar=d_all[:, bass.ds(C * at + c, 1)], in1=scaled[:, c, :],
                                                       op0=ALU.mult, op1=ALU.add).then_inc(acc_free, 1)
                    dve.wait_ge(acc_free, C * (ph.acc_before + row + 2))
                    nc.vector.tensor_tensor(result[:, :, :], scaled[:, :, :], base_in[:, :, :],
                                            ALU.add).then_inc(out_ready, 1)

        @block.tensor
        def _(pe):
            pe.sem_inc(tile_used, C)
            pe.wait_ge(const_ready, 1)
            pe.wait_ge(const_in, 32)

            def products(ph, kind, body, t0, i):
                t = t0 + i * kind.count("T")
                for s in [s for s, what in enumerate(kind) if what == "T"]:
                    for b in range(C):
                        k = C * (ph.t_first + t) + b
                        pe.wait_ge(dve_done, AHEAD + C * (BODY * body + s) + b + 1)
                        for c in range(C):
                            hi = a_hi[:, b, P * c:P * c + P]
                            lo = a_lo[:, b, P * c:P * c + P]
                            if ph.second:
                                Gk = G[:, bass.ds(k, 1), :]
                                pe_mm(acc[:, c, 0:F], hi, Gk[:, :, 0:F])
                                pe_mm(acc[:, c, F:2 * F], hi, Gk[:, :, F + 2:GW])
                                last = pe_mm(acc[:, c, 0:F], lo, Gk[:, :, 0:F])
                            else:
                                Gk = G[:, bass.ds(k, 1), :]
                                pe_mm(acc[:, c, 0:SUMMED], hi, Gk[:, :, 0:SUMMED])
                                pe_mm(acc[:, c, 0:F], hi, Gk[:, :, F + 2:GW])
                                last = pe_mm(acc[:, c, 0:SUMMED], lo, Gk[:, :, 0:SUMMED])
                        last.then_inc(tile_used, 1)
                    t = t + 1
                return last

            def pe_mm(out, stationary, moving, start=False):
                return nc.tensor.matmul(out, stationary, moving, start=start, stop=False, skip_group_check=True)

            def open_banks(count):
                for c in range(C):
                    pe.wait_ge(acc_free, count + c + 1)
                    pe_mm(acc[:, c, 0:2], zeros[:, :], zeros[:, 0:2], start=True)

            for ph in FIRST:
                with pe.Fori(0, GROUP) as row:
                    at = ph.rows_before + row
                    pe.wait_ge(h_ready, at + 1)
                    for k in range(2):
                        for c in range(C):
                            last = nc.tensor.transpose(tr_ps[:, k, P * c:P * c + P], h[:, c, P * k:P * k + P], ident[:, :])
                    last.then_inc(tr_ready, 1)
                    if ph.t_units:
                        open_banks(C * (ph.acc_before + row))
                        if ph.group:
                            pe.wait_ge(G_ready, GROUP * ph.group)
                    parts = list(ph.parts())
                    for j, (kind, count, body0, t0, n0) in enumerate(parts):
                        if "T" in kind:
                            with pe.Fori(0, count) as i:
                                products(ph, kind, ph.bodies_before + ph.bodies * row + body0 + i, t0, i)
                        if j == 0:
                            pe.wait_ge(ht_ready, at + 1)
                            pe.wait_ge(g_used, at + 1)
                            for c in range(C):
                                for k in range(2):
                                    last = nc.tensor.matmul(g_ps[:, c // 2, F * (c % 2):F * (c % 2) + F],
                                                            h_t[:, k, P * c:P * c + P], wt[:, k, :],
                                                            start=(k == 0), stop=(k == 1))
                            last.then_inc(g_ready, 1)
            pe.wait_ge(G_ready, BLOCKS)
            for ph in SECOND:
                with pe.Fori(0, GROUP) as row:
                    open_banks(C * (ph.acc_before + row))
                    for kind, count, body0, t0, n0 in ph.parts():
                        with pe.Fori(0, count) as i:
                            products(ph, kind, ph.bodies_before + ph.bodies * row + body0 + i, t0, i)


def kernel(x, adj, L0_gnn_W, L0_gnn_b):
    import numpy as np
    import concourse.bacc as bacc
    from concourse.bass_utils import run_bass_kernel_spmd

    x, adj = np.asarray(x), np.asarray(adj)
    W, b = np.asarray(L0_gnn_W), np.asarray(L0_gnn_b)
    x_rows = np.ascontiguousarray(x.reshape(BLOCKS, C, P, F).transpose(0, 2, 1, 3))
    adj_t = np.ascontiguousarray(adj.reshape(BLOCKS, R, BLOCKS, C, P).transpose(0, 2, 4, 3, 1))
    adj_n = np.ascontiguousarray(adj.reshape(BLOCKS, C, P, BLOCKS, R).transpose(0, 3, 2, 1, 4))
    w_t = np.ascontiguousarray(W.T.reshape(2, P, F).transpose(1, 0, 2))
    bias = np.ascontiguousarray(b.reshape(1, F))
    given = {"x_rows": x_rows, "adj_t": adj_t, "adj_n": adj_n, "w_t": w_t, "bias": bias}

    nc = bacc.Bacc("TRN2", target_bir_lowering=False, num_devices=1)
    args = [nc.dram_tensor(name, a.shape, mybir.dt.from_np(a.dtype), kind="ExternalInput").ap()
            for name, a in given.items()]
    out = nc.dram_tensor("out_rows", x_rows.shape, mybir.dt.float32, kind="ExternalOutput").ap()
    gnn_kernel(nc, *args, out)
    r = run_bass_kernel_spmd(nc, [given], core_ids=[0])
    got = r.results[0]["out_rows"]
    return np.ascontiguousarray(got.transpose(0, 2, 1, 3).reshape(N, F))
```

```python
from contextlib import ExitStack

import concourse.bass as bass
from concourse import mybir


P = 128
N = 8192
F = 256
R = 512
C = R // P
BLOCKS = N // R
GROUP = 4
GROUPS = BLOCKS // GROUP
BODY = 4
AHEAD = C * BODY
ROW_BODIES = BLOCKS // BODY
LN_EPS = 1e-5
GW = 2 * F + 2
SUMMED = F + 2

SUM4, MIX4, MUL4 = "NNNN", "TNTN", "TTTT"
PASS1_LOOPS = [[(SUM4, 2), (SUM4, 2)], [(MIX4, 1), (MIX4, 1), (SUM4, 2)],
               [(MIX4, 2), (MIX4, 2)], [(MIX4, 2), (MUL4, 2)]]


class Phase:

    def __init__(self, second, group, loops, bodies_before, t_before, rows_before, acc_before):
        self.second, self.group, self.loops = second, group, loops
        self.row0 = GROUP * group
        self.bodies = sum(n for _, n in loops)
        self.t_units = sum(kind.count("T") * n for kind, n in loops)
        self.n_units = sum(kind.count("N") * n for kind, n in loops)
        self.t_first = GROUP * group if second else 0
        self.n_first = GROUP * group
        self.bodies_before, self.t_before = bodies_before, t_before
        self.rows_before, self.acc_before = rows_before, acc_before

    def loop(self, k, row):
        found = []
        for j in (range(1) if k == 0 else range(1, len(self.loops))):
            before = self.loops[:j]
            found.append((*self.loops[j], self.bodies_before + self.bodies * row + sum(n for _, n in before),
                          sum(n * what.count("T") for what, n in before),
                          sum(n * what.count("N") for what, n in before)))
        return found

    def at(self, row):
        return self.row0 + row


def phases():
    found, bodies, t, rows, acc = [], 0, 0, 0, 0
    plans = [(False, g, PASS1_LOOPS[g]) for g in range(GROUPS)]
    plans += [(True, g, [(MUL4, 1), (MUL4, GROUPS - g - 1)][:GROUPS - g]) for g in range(GROUPS)]
    for second, g, loops in plans:
        ph = Phase(second, g, loops, bodies, t, rows, acc)
        found.append(ph)
        bodies += GROUP * ph.bodies
        t += GROUP * ph.t_units
        rows += GROUP
        acc += GROUP if ph.t_units else 0
    return found


def each_row(eng, plan, step):
    for ph, behind in zip(plan, [*plan[1:], None]):
        with eng.Fori(0, GROUP - 1) as row:
            step(ph, row, ph, row + 1)
        step(ph, GROUP - 1, behind, 0)


def gnn_kernel(nc, x_rows, adj_t, adj_n, w_t, bias, out_rows):
    f32, f32r = mybir.dt.float32, mybir.dt.float32r
    ALU, ACT, AX = mybir.AluOpType, mybir.ActivationFunctionType, mybir.AxisListType.X
    PHASES = phases()
    FIRST, SECOND = PHASES[:GROUPS], PHASES[GROUPS:]
    base_dram = nc.dram_tensor("base_dram", (BLOCKS, P, C, F), f32)

    ctx = ExitStack()
    with ctx:
        def sb(name, shape, dt=f32):
            return ctx.enter_context(nc.sbuf_tensor(name, shape, dt))

        def pb(name, shape):
            return ctx.enter_context(nc.psum_tensor(name, shape, f32))

        def sem(name):
            return ctx.enter_context(nc.semaphore(name))

        G = sb("G", [P, N // P, GW], f32r)
        raw = [sb(f"raw{s}", [P, C, R]) for s in range(BODY)]
        a_hi = sb("a_hi", [P, C, R], f32r)
        a_lo = sb("a_lo", [P, C, R], f32r)
        wt = sb("wt", [P, 2, F])
        bias_all = sb("bias_all", [P, F])
        ident = sb("ident", [P, P])
        zeros = sb("zeros", [P, P], f32r)
        minus_half = sb("minus_half", [P, C])
        x_in = sb("x_in", [P, C, F])
        x_bias = sb("x_bias", [P, C, F])
        h = sb("h", [P, C, F])
        h_t = sb("h_t", [P, 2, R])
        stats = sb("stats", [P, C, 6])
        meanvar = sb("meanvar", [P, C, 2])
        var_eps = sb("var_eps", [P, C])
        rstd = sb("rstd", [P, C])
        newton = sb("newton", [P, C])
        sums = sb("sums", [P, C, BLOCKS])
        total = sb("total", [P, C])
        d_row = sb("d_row", [P, C])
        d_all = sb("d_all", [P, N // P])
        part = sb("part", [P, C, SUMMED])
        g_all = sb("g_all", [P, C, F])
        base_in = x_in
        scaled = h
        result = g_all

        acc = pb("acc", [P, 2 * C, 512])
        tr_ps = acc[:, C:C + 2, :]
        g_ps = acc[:, C + 2:C + 4, :]

        raw_in = [sem(f"raw_in{s}") for s in range(BODY)]
        act_done = sem("act_done")
        dve_done = sem("dve_done")
        tile_used = sem("tile_used")
        const_in = sem("const_in")
        ident0 = sem("ident0")
        const_ready = sem("const_ready")
        x_here = sem("x_here")
        x_free = sem("x_free")
        stats_ready = sem("stats_ready")
        pool_step = sem("pool_step")
        h_ready = sem("h_ready")
        tr_ready = sem("tr_ready")
        ht_ready = sem("ht_ready")
        g_ready = sem("g_ready")
        g_used = sem("g_used")
        act_sums = sem("act_sums")
        sums_free = sem("sums_free")
        total_ready = sem("total_ready")
        d_ready = sem("d_ready")
        stats_step = sem("stats_step")
        g_added = sem("g_added")
        G_ready = sem("G_ready")
        base_ready = sem("base_ready")
        base_stored = sem("base_stored")
        base_here = sem("base_here")
        acc_free = sem("acc_free")
        scaled_ready = sem("scaled_ready")
        out_ready = sem("out_ready")
        out_stored = sem("out_stored")

        pool_gate = sem("pool_gate")
        dve_gate = sem("dve_gate")

        def gate(eng, signal):
            eng.sem_inc(signal, 1)

        block = ctx.enter_context(nc.Block())

        @block.sync
        def _(sp):
            sp.dma_start(wt[:, :, :], w_t).then_inc(const_in, 16)
            sp.dma_start(bias_all[:, :], bias[0:1, :].broadcast_to([P, F])).then_inc(const_in, 16)

            def load(ph, row, kind, body, t0, n0, i):
                t, n = t0 + i * kind.count("T"), n0 + i * kind.count("N")
                for s, what in enumerate(kind):
                    unit = BODY * body + s
                    sp.wait_ge(act_done, C * unit + C)
                    sp.wait_ge(dve_done, C * unit + C)
                    if what == "T":
                        src = adj_t[bass.ds(ph.at(row), 1), bass.ds(ph.t_first + t, 1), :, :, :]
                        t = t + 1
                    else:
                        src = adj_n[bass.ds(ph.at(row), 1), bass.ds(ph.n_first + n, 1), :, :, :]
                        n = n + 1
                    sp.dma_start(raw[s][:, :, :], src.rearrange("a b p c j -> (a b p) c j")).then_inc(raw_in[s], 16)

            for ph in PHASES:
                with sp.Fori(0, GROUP) as row:
                    if not ph.second:
                        sp.wait_ge(x_free, ph.at(row) + 1)
                        sp.dma_start(x_in[:, :, :], x_rows[bass.ds(ph.at(row), 1), :, :, :].rearrange(
                            "a p c f -> (a p) c f")).then_inc(x_here, 16)
                    for k in range(2):
                        for kind, count, body, t0, n0 in ph.loop(k, row):
                            with sp.Fori(0, count) as i:
                                load(ph, row, kind, body + i, t0, n0, i)

        @block.gpsimd
        def _(pool):
            pool.memset(ident[:, :], 0.0).then_inc(ident0, 1)
            pool.memset(minus_half[:, :], -0.5)
            pool.memset(zeros[:, :].bitcast(f32), 0.0)
            pool.memset(G[:, :, F:F + 2].bitcast(f32), 1.0)
            pool.wait_ge(ident0, 1)
            pool.affine_select(out=ident[:, :], in_=ident[:, :], compare_op=ALU.not_equal, fill=1.0, base=0,
                               pattern=[[-1, P]], channel_multiplier=1).then_inc(const_ready, 1)
            pool.wait_ge(const_ready, 1)
            pool.wait_ge(const_in, 32)
            NORM_STEPS, ROW_STEPS = 6, 10

            def rsqrt(step, out, v):
                step(pool.tensor_tensor(out, v, minus_half[:, :], ALU.pow))
                step(pool.tensor_tensor(newton[:, :], out, out, ALU.mult))
                step(pool.tensor_tensor(newton[:, :], newton[:, :], v, ALU.mult))
                step(pool.tensor_scalar(newton[:, :], newton[:, :], -0.5, 1.5, ALU.mult, ALU.add))
                return pool.tensor_tensor(out, out, newton[:, :], ALU.mult)

            bias_c = bias_all[:, :].rearrange("p (a f) -> p a f", a=1).broadcast_to([P, C, F])

            def normalise(at, step, first_one=False):
                pool.wait_ge(stats_ready, at + 1)
                gate(pool, pool_gate)
                step(pool.tensor_scalar(var_eps[:, :], meanvar[:, :, 1], LN_EPS, None, ALU.add))
                step(rsqrt(step, rstd[:, :], var_eps[:, :]))
                if not first_one:
                    pool.wait_ge(tr_ready, at)
                    gate(pool, pool_gate)
                for c in range(C):
                    last = pool.tensor_scalar(h[:, c, :], x_in[:, c, :], meanvar[:, c, 0:1], rstd[:, c:c + 1],
                                              ALU.subtract, ALU.mult)
                last.then_inc(h_ready, 1)

            def add_bias():
                pool.tensor_tensor(x_bias[:, :, :], x_in[:, :, :], bias_c, ALU.add).then_inc(x_free, 1)

            def first(ph, row, behind, row_behind):
                done = [0]
                at = ph.at(row)

                def step(ins):
                    done[0] += 1
                    ins.then_inc(pool_step, 1)
                    pool.wait_ge(pool_step, NORM_STEPS + at * ROW_STEPS + done[0])
                    gate(pool, pool_gate)

                pool.wait_ge(total_ready, at + 1)
                rsqrt(step, d_row[:, :], total[:, :]).then_inc(d_ready, 1)
                if not behind.second:
                    normalise(behind.at(row_behind), step)
                pool.wait_ge(base_ready, at + 1)
                gate(pool, pool_gate)
                pool.dma_start(base_dram[bass.ds(at, 1), :, :, :].rearrange("a p c f -> (a p) c f"),
                               x_bias[:, :, :]).then_inc(base_stored, 16)
                pool.wait_ge(base_stored, 16 * at + 16)
                if not behind.second:
                    add_bias()
                    assert done[0] == ROW_STEPS

            def second(ph, row, behind, row_behind):
                at = ph.at(row)
                pool.wait_ge(out_ready, at + 1)
                gate(pool, pool_gate)
                pool.dma_start(base_in[:, :, :], base_dram[bass.ds(at, 1), :, :, :].rearrange(
                    "a p c f -> (a p) c f")).then_inc(base_here, 16)
                pool.wait_ge(out_ready, at + 2)
                gate(pool, pool_gate)
                pool.dma_start(out_rows[bass.ds(at, 1), :, :, :].rearrange("a p c f -> (a p) c f"),
                               result[:, :, :]).then_inc(out_stored, 16)
                pool.wait_ge(out_stored, 16 * at + 16)

            at_start = [0]

            def start_step(ins):
                at_start[0] += 1
                ins.then_inc(pool_step, 1)
                pool.wait_ge(pool_step, at_start[0])

            normalise(0, start_step, True)
            add_bias()
            assert at_start[0] == NORM_STEPS
            each_row(pool, PHASES, lambda ph, *rest: (second if ph.second else first)(ph, *rest))

        @block.scalar
        def _(act):
            act.sem_inc(act_done, AHEAD)

            def units(ph, row, kind, body, t0, n0, i):
                t = ph.t_before + ph.t_units * row + t0 + i * kind.count("T")
                n = n0 + i * kind.count("N")
                for s, what in enumerate(kind):
                    act.wait_ge(raw_in[s], 16 * (body + 1))
                    if what == "T":
                        for b in range(C):
                            act.wait_ge(tile_used, C * t + b + 1)
                            nc.scalar.copy(a_hi[:, b, :], raw[s][:, b, :]).then_inc(act_done, 1)
                        t = t + 1
                    else:
                        for c in range(C // 2):
                            nc.scalar.activation(raw[s][:, c, :], raw[s][:, c, :], ACT.Copy,
                                                 accum_out=sums[:, c, bass.ds(n, 1)]).then_inc(act_done, 2)
                        n = n + 1

            def loops(ph, row, k):
                for kind, count, body, t0, n0 in ph.loop(k, row):
                    if k == 0 and not ph.second:
                        act.wait_ge(sums_free, ph.at(row) + 1)
                    with act.Fori(0, count) as i:
                        units(ph, row, kind, body + i, t0, n0, i)

            def step(ph, row, behind, row_behind):
                at = ph.at(row)
                loops(ph, row, 1)
                if not ph.second:
                    act.wait_ge(tr_ready, at + 1)
                    nc.scalar.activation(h_t[:, 0, :], tr_ps[:, 0, :], ACT.Relu)
                    nc.scalar.activation(h_t[:, 1, :], tr_ps[:, 1, :], ACT.Relu).then_inc(ht_ready, 1)
                if behind:
                    loops(behind, row_behind, 0)
                if ph.second:
                    act.wait_ge(tile_used, C * (ph.t_before + ph.t_units * (row + 1)) + C)
                    act.wait_ge(out_ready, at + 1)
                    for c in range(C):
                        nc.scalar.activation(scaled[:, c, :], acc[:, bass.ds(C * (row % 2) + c, 1), F:2 * F], ACT.Copy,
                                             scale=d_all[:, bass.ds(C * at + c, 1)]).then_inc(scaled_ready, 1)

            loops(PHASES[0], 0, 0)
            each_row(act, PHASES, step)

        @block.vector
        def _(dve):
            dve.sem_inc(dve_done, AHEAD)
            dve.sem_inc(acc_free, C)
            for buffer_free in (x_free, g_used, sums_free, out_ready):
                dve.sem_inc(buffer_free, 1)

            def units(ph, row, kind, body, t0, n0, i):
                n = n0 + i * kind.count("N")
                for s, what in enumerate(kind):
                    if what == "T":
                        for b in range(C):
                            dve.wait_ge(act_done, AHEAD + C * (BODY * body + s) + b + 1)
                            nc.vector.tensor_tensor(a_lo[:, b, :], raw[s][:, b, :], a_hi[:, b, :].bitcast(f32),
                                                    ALU.subtract).then_inc(dve_done, 1)
                    else:
                        dve.wait_ge(raw_in[s], 16 * (body + 1))
                        nc.vector.tensor_reduce(sums[:, C // 2:C, bass.ds(n, 1)], raw[s][:, C // 2:C, :], AX,
                                                ALU.add).then_inc(dve_done, C)
                        n = n + 1

            def loops(ph, row, k):
                for kind, count, body, t0, n0 in ph.loop(k, row):
                    with dve.Fori(0, count) as i:
                        units(ph, row, kind, body + i, t0, n0, i)

            def statistics(at):
                dve.wait_ge(x_here, 16 * at + 16)
                for c in range(C):
                    last = nc.vector.bn_stats(stats[:, c, :], x_in[:, c, :])
                last.then_inc(stats_step, 1)
                dve.wait_ge(stats_step, at + 1)
                gate(dve, dve_gate)
                for c in range(C):
                    last = nc.vector.bn_aggr(meanvar[:, c, :], stats[:, c, :])
                last.then_inc(stats_ready, 1)

            def row_sums(ph, row):
                row_done = AHEAD + C * BODY * (ph.bodies_before + ph.bodies * (row + 1))
                dve.wait_ge(act_done, row_done)
                dve.wait_ge(dve_done, row_done)
                nc.vector.tensor_reduce(total[:, :], sums[:, :, 0:ph.n_units], AX, ALU.add).then_inc(sums_free, 1)
                dve.wait_ge(sums_free, ph.at(row) + 2)
                if ph.t_units:
                    dve.wait_ge(tile_used, C * (ph.t_before + ph.t_units * (row + 1)) + C)
                    for c in range(C):
                        nc.vector.tensor_copy(part[:, c, :], acc[:, c, 0:SUMMED]).then_inc(acc_free, 1)
                    dve.wait_ge(acc_free, C * (ph.acc_before + row + 2))
                    nc.vector.scalar_tensor_tensor(out=total[:, :], in0=part[:, :, F], scalar=1.0, in1=total[:, :],
                                                   op0=ALU.add, op1=ALU.add).then_inc(total_ready, 1)
                else:
                    nc.vector.tensor_scalar(total[:, :], total[:, :], 1.0, None, ALU.add).then_inc(total_ready, 1)

            def finish_first(ph, row):
                at = ph.at(row)
                dve.wait_ge(d_ready, at + 1)
                nc.vector.tensor_copy(d_all[:, bass.ds(C * at, C)], d_row[:, :])
                dve.wait_ge(g_ready, at + 1)
                for c in range(C):
                    g_c = g_ps[:, c // 2, F * (c % 2):F * (c % 2) + F]
                    nc.vector.tensor_scalar(g_all[:, c, :], g_c, d_row[:, c:c + 1], None, ALU.mult)
                    last = nc.vector.tensor_scalar(G[:, bass.ds(C * at + c, 1), 0:F], g_c, d_row[:, c:c + 1], None, ALU.mult)
                last.then_inc(g_used, 1)
                dve.wait_ge(g_used, at + 2)
                nc.vector.tensor_tensor(G[:, bass.ds(C * at, C), F + 2:GW], g_all[:, :, :],
                                        G[:, bass.ds(C * at, C), 0:F].bitcast(f32), ALU.subtract).then_inc(G_ready, 1)
                if ph.t_units:
                    nc.vector.tensor_tensor(g_all[:, :, :], g_all[:, :, :], part[:, :, 0:F], ALU.add).then_inc(g_added, 1)
                    dve.wait_ge(g_added, ph.acc_before + row + 1)
                dve.wait_ge(x_free, at + 2)
                for c in range(C):
                    last = nc.vector.scalar_tensor_tensor(out=x_bias[:, c, :], in0=g_all[:, c, :],
                                                          scalar=d_row[:, c:c + 1], in1=x_bias[:, c, :],
                                                          op0=ALU.mult, op1=ALU.add)
                last.then_inc(base_ready, 1)

            def finish_second(ph, row):
                at = ph.at(row)
                dve.wait_ge(base_here, 16 * at + 16)
                for c in range(C):
                    dve.wait_ge(scaled_ready, C * at + c + 1)
                    nc.vector.scalar_tensor_tensor(out=scaled[:, c, :], in0=acc[:, bass.ds(C * (row % 2) + c, 1), 0:F],
                                                   scalar=d_all[:, bass.ds(C * at + c, 1)], in1=scaled[:, c, :],
                                                   op0=ALU.mult, op1=ALU.add).then_inc(acc_free, 1)
                dve.wait_ge(acc_free, C * (ph.acc_before + row + 2))
                nc.vector.tensor_tensor(result[:, :, :], scaled[:, :, :], base_in[:, :, :],
                                        ALU.add).then_inc(out_ready, 1)

            def step(ph, row, behind, row_behind):
                loops(ph, row, 1)
                if not ph.second:
                    row_sums(ph, row)
                    if not behind.second:
                        statistics(behind.at(row_behind))
                if behind:
                    loops(behind, row_behind, 0)
                (finish_second if ph.second else finish_first)(ph, row)

            statistics(0)
            loops(PHASES[0], 0, 0)
            each_row(dve, PHASES, step)

        @block.tensor
        def _(pe):
            pe.sem_inc(tile_used, C)
            pe.wait_ge(const_ready, 1)
            pe.wait_ge(const_in, 32)

            def mm(out, stationary, moving, start=False):
                return nc.tensor.matmul(out, stationary, moving, start=start, stop=False, skip_group_check=True)

            def open_banks(bank, freed):
                for c in range(C):
                    pe.wait_ge(acc_free, freed + c + 1)
                    mm(acc[:, bank + c, 0:2], zeros[:, :], zeros[:, 0:2], start=True)

            def products(ph, kind, bank, body, t):
                for s in [s for s, what in enumerate(kind) if what == "T"]:
                    for b in range(C):
                        Gb = G[:, bass.ds(C * (ph.t_first + t) + b, 1), :]
                        pe.wait_ge(dve_done, AHEAD + C * (BODY * body + s) + b + 1)
                        for c in range(C):
                            hi, lo = a_hi[:, b, P * c:P * c + P], a_lo[:, b, P * c:P * c + P]
                            if ph.second:
                                mm(acc[:, bank + c, 0:F], hi, Gb[:, :, 0:F])
                                mm(acc[:, bank + c, F:2 * F], hi, Gb[:, :, F + 2:GW])
                                last = mm(acc[:, bank + c, 0:F], lo, Gb[:, :, 0:F])
                            else:
                                mm(acc[:, c, 0:SUMMED], hi, Gb[:, :, 0:SUMMED])
                                mm(acc[:, c, 0:F], hi, Gb[:, :, F + 2:GW])
                                last = mm(acc[:, c, 0:SUMMED], lo, Gb[:, :, 0:SUMMED])
                        last.then_inc(tile_used, 1)
                    t = t + 1

            def loops(ph, row, k, bank):
                for kind, count, body, t0, n0 in ph.loop(k, row):
                    if "T" in kind:
                        with pe.Fori(0, count) as i:
                            products(ph, kind, bank, body + i, t0 + i * kind.count("T"))

            for ph in FIRST:
                if ph.group:
                    pe.wait_ge(G_ready, GROUP * ph.group - 1)
                with pe.Fori(0, GROUP) as row:
                    at = ph.at(row)
                    if ph.t_units:
                        open_banks(0, C * (ph.acc_before + row))
                    loops(ph, row, 0, 0)
                    pe.wait_ge(h_ready, at + 1)
                    for k in range(2):
                        for c in range(C):
                            last = nc.tensor.transpose(tr_ps[:, k, P * c:P * c + P], h[:, c, P * k:P * k + P], ident[:, :])
                    last.then_inc(tr_ready, 1)
                    if ph.group:
                        pe.wait_ge(G_ready, GROUP * ph.group)
                    loops(ph, row, 1, 0)
                    pe.wait_ge(ht_ready, at + 1)
                    pe.wait_ge(g_used, at + 1)
                    for c in range(C):
                        for k in range(2):
                            last = nc.tensor.matmul(g_ps[:, c // 2, F * (c % 2):F * (c % 2) + F],
                                                    h_t[:, k, P * c:P * c + P], wt[:, k, :],
                                                    start=(k == 0), stop=(k == 1))
                    last.then_inc(g_ready, 1)
            pe.wait_ge(acc_free, C * (SECOND[0].acc_before + 1))
            for ph in SECOND:
                with pe.Fori(0, GROUP // 2) as pair:
                    for side in range(2):
                        row = 2 * pair + side
                        open_banks(C * side, C * (ph.acc_before + row - 1))
                        loops(ph, row, 0, C * side)
                        pe.wait_ge(G_ready, BLOCKS)
                        loops(ph, row, 1, C * side)


def kernel(x, adj, L0_gnn_W, L0_gnn_b):
    import numpy as np
    import concourse.bacc as bacc
    from concourse.bass_utils import run_bass_kernel_spmd

    x, adj = np.asarray(x), np.asarray(adj)
    W, b = np.asarray(L0_gnn_W), np.asarray(L0_gnn_b)
    x_rows = np.ascontiguousarray(x.reshape(BLOCKS, C, P, F).transpose(0, 2, 1, 3))
    adj_t = np.ascontiguousarray(adj.reshape(BLOCKS, R, BLOCKS, C, P).transpose(0, 2, 4, 3, 1))
    adj_n = np.ascontiguousarray(adj.reshape(BLOCKS, C, P, BLOCKS, R).transpose(0, 3, 2, 1, 4))
    w_t = np.ascontiguousarray(W.T.reshape(2, P, F).transpose(1, 0, 2))
    bias = np.ascontiguousarray(b.reshape(1, F))
    given = {"x_rows": x_rows, "adj_t": adj_t, "adj_n": adj_n, "w_t": w_t, "bias": bias}

    nc = bacc.Bacc("TRN2", target_bir_lowering=False, num_devices=1)
    args = [nc.dram_tensor(name, a.shape, mybir.dt.from_np(a.dtype), kind="ExternalInput").ap()
            for name, a in given.items()]
    out = nc.dram_tensor("out_rows", x_rows.shape, mybir.dt.float32, kind="ExternalOutput").ap()
    gnn_kernel(nc, *args, out)
    r = run_bass_kernel_spmd(nc, [given], core_ids=[0])
    got = r.results[0]["out_rows"]
    return np.ascontiguousarray(got.transpose(0, 2, 1, 3).reshape(N, F))
```

```python
from contextlib import ExitStack

import concourse.bass as bass
from concourse import mybir


P = 128
N = 8192
F = 256
R = 512
C = R // P
HALF = C // 2
BLOCKS = N // R
AHEAD = 7
OWN = BLOCKS - AHEAD
SLOTS = 4
LN_EPS = 1e-5
SUMMED = F + 2
GW = 2 * SUMMED

SUM2 = [("N", 0, 0), ("N", 0, 1), ("N", 1, 0), ("N", 1, 1)]
MUL1 = [("T", 0, 0), ("T", 0, 1)]
MUL2 = [("T", 0, 0), ("T", 0, 1), ("T", 1, 0), ("T", 1, 1)]
MIX1 = [("T", 0, 0), ("N", 0, 0), ("T", 0, 1), ("N", 0, 1)]
MIX2 = [(what, unit, half) for unit in (0, 1) for half in (0, 1) for what in "TN"]
MUL1_MIX2 = MUL1 + [(what, unit + 1 if what == "T" else unit, half) for what, unit, half in MIX2]
MIX1_MIX2 = MIX1 + [(what, unit + 1, half) for what, unit, half in MIX2]

GROUPS = [
    (0, 1, [(SUM2, 1), (SUM2, 2), (SUM2, 1), (SUM2, 1), (SUM2, 3)]),
    (1, 1, [(SUM2, 1), (SUM2, 2), (MIX1, 1), (SUM2, 1), (SUM2, 3)]),
    (2, 1, [(SUM2, 1), (SUM2, 2), (MIX2, 1), (SUM2, 1), (SUM2, 2)]),
    (3, 1, [(MIX2, 1), (SUM2, 2), (MIX1, 1), (SUM2, 1), (SUM2, 2)]),
    (4, 1, [(MIX2, 1), (SUM2, 1), (MIX2, 1), (SUM2, 1), (SUM2, 2)]),
    (5, 1, [(MIX2, 1), (MIX2, 1), (MIX1, 1), (SUM2, 1), (SUM2, 2)]),
    (6, 1, [(MIX2, 1), (SUM2, 1), (MIX2, 1), (SUM2, 1), (MIX2, 1)]),
    (7, 1, [(MIX1, 1), (MIX1_MIX2, 1), (MIX2, 1), (MIX1, 1), (SUM2, 1)]),
    (8, 1, [(MIX1, 1), (MIX1_MIX2, 1), (MIX2, 2)]),
    (9, 1, [(MIX1, 1), (MIX1_MIX2, 1), (MUL2, 1), (MIX2, 1), (MIX1, 1)]),
    (10, 2, [(MUL1, 1), (MUL1_MIX2, 1), (MUL2, 1), (MIX2, 2)]),
    (12, 4, [(MUL1, 1), (MUL1_MIX2, 1), (MUL2, 1), (MIX2, 1), (MUL2, 2)]),
]


def units_of(what, kind):
    return sum(w == what for w, _, _ in kind) // 2


class Loop:

    def __init__(self, kind, count, halves, t, n, first_slot, first_split):
        self.kind, self.count = kind, count
        self.halves, self.t, self.n = halves, t, n
        self.first_slot = first_slot
        self.first_split = first_split

    def slot(self, s):
        return (self.first_slot + s) % SLOTS

    def came(self, halves, s):
        return 16 // SLOTS * (halves + s - self.slot(s)) + 16

    def split(self, unit, half):
        return HALF * ((self.first_split + unit) % 2) + half


class Phase:

    def __init__(self, second, row0, rows, loops, halves_before, t_before, acc_before):
        self.second, self.row0, self.rows = second, row0, rows
        self.loops = loops = [(kind, n) for kind, n in loops if n]
        self.halves = sum(n * len(kind) for kind, n in loops)
        self.t_units = sum(n * units_of("T", kind) for kind, n in loops)
        self.n_units = sum(n * units_of("N", kind) for kind, n in loops)
        self.kept_busy = loops[0][0] in (MUL1, MIX1)
        assert self.t_units == (BLOCKS - row0 if second else row0)
        assert self.n_units == (0 if second else BLOCKS - row0)
        self.t_first = row0 if second else 0
        self.halves_before, self.t_before, self.acc_before = halves_before, t_before, acc_before
        self.own = row0 + min(row0, AHEAD) if not second and row0 < OWN else None
        self.ahead = 2 * row0 + 1 if not second and row0 < AHEAD else None
        self.normalised = BLOCKS if self.own is None else self.own + (1 if self.ahead is None else 2)
        assert rows == 1 or self.own is None
        self.alternate = second or row0 > OWN
        assert rows == 1 or self.halves % SLOTS == self.t_units % 2 == row0 % 2 == rows % 2 == 0
        assert all(n == 1 or (len(kind) % SLOTS == 0 and units_of("T", kind) % 2 == 0) for kind, n in loops)

    def loop(self, k, row):
        found = []
        for j in range(min(k, len(self.loops)), len(self.loops) if k == 4 else min(k + 1, len(self.loops))):
            before = self.loops[:j]
            halves = self.halves_before + sum(n * len(kind) for kind, n in before)
            t = sum(n * units_of("T", kind) for kind, n in before)
            found.append(Loop(*self.loops[j], halves + self.halves * row, t,
                              sum(n * units_of("N", kind) for kind, n in before),
                              halves % SLOTS, (self.t_before + t) % 2))
        return found

    def at(self, row):
        return self.row0 + row

    def side(self, row):
        if not self.alternate:
            return 0
        return (self.row0 - OWN) % 2 if self.rows == 1 else (row + (self.row0 - OWN)) % 2

    def halves_used(self, row):
        return SLOTS + 2 * (self.t_before + self.t_units * (row + 1))


def second_loops(units):
    return [(MUL1, 1), (MUL1, 1), (MUL2, 1), (MUL2, units // 2 - 2), (MUL1, units % 2)]


def phases():
    found, halves, t, acc = [], 0, 0, 0
    plans = [(False, row0, rows, loops) for row0, rows, loops in GROUPS]
    plans += [(True, row0, rows, second_loops(BLOCKS - row0)) for row0, rows, _ in GROUPS]
    for second, row0, rows, loops in plans:
        ph = Phase(second, row0, rows, loops, halves, t, acc)
        found.append(ph)
        halves += rows * ph.halves
        t += rows * ph.t_units
        acc += rows if ph.t_units else 0
    return found


def each_row(eng, plan, step):
    for ph, behind in zip(plan, [*plan[1:], None]):
        if ph.rows > 2:
            with eng.Fori(0, ph.rows - 1) as row:
                step(ph, row, ph, row + 1)
        elif ph.rows == 2:
            step(ph, 0, ph, 1)
        step(ph, ph.rows - 1, behind, 0)


def gnn_kernel(nc, x_rows, adj_t, adj_n, w_t, bias, out_rows):
    f32, f32r = mybir.dt.float32, mybir.dt.float32r
    ALU, ACT, AX = mybir.AluOpType, mybir.ActivationFunctionType, mybir.AxisListType.X
    PHASES = phases()
    FIRST, SECOND = PHASES[:len(GROUPS)], PHASES[len(GROUPS):]
    base_dram = nc.dram_tensor("base_dram", (BLOCKS, P, C, F), f32)

    ctx = ExitStack()
    with ctx:
        def sb(name, shape, dt=f32):
            return ctx.enter_context(nc.sbuf_tensor(name, shape, dt))

        def pb(name, shape):
            return ctx.enter_context(nc.psum_tensor(name, shape, f32))

        def sem(name):
            return ctx.enter_context(nc.semaphore(name))

        G = sb("G", [P, N // P, GW], f32r)
        raw = [sb(f"raw{s}", [P, HALF, R]) for s in range(SLOTS)]
        a_hi = sb("a_hi", [P, SLOTS, HALF, R], f32r)
        a_lo = sb("a_lo", [P, SLOTS, HALF, R], f32r)
        wt = sb("wt", [P, 2, F])
        bias_all = sb("bias_all", [P, F])
        ident = sb("ident", [P, P])
        zeros = sb("zeros", [P, P], f32r)
        minus_half = sb("minus_half", [P, C])
        x_own = sb("x_own", [P, C, F])
        x_ahead = sb("x_ahead", [P, C, F])
        h = sb("h", [P, C, F])
        h_t = sb("h_t", [P, 2, R])
        stats = sb("stats", [P, C, 6])
        meanvar = sb("meanvar", [P, 2, C, 2])
        var_eps = sb("var_eps", [P, C])
        rstd = sb("rstd", [P, C])
        newton = sb("newton", [P, C])
        sums = sb("sums", [P, C, BLOCKS])
        total = sb("total", [P, C])
        d_row = sb("d_row", [P, C])
        d_all = sb("d_all", [P, N // P])
        part = sb("part", [P, C, SUMMED])
        g_all = sb("g_all", [P, C, F])
        g_joint = h
        base_in = x_own
        x_again = x_ahead
        base_out = part[:, :, 0:F]
        base = part[:, :, 0:F]
        scaled = h
        result = g_all

        acc = pb("acc", [P, 2 * C, 512])
        tr_ps = acc[:, C:C + 2, :]
        g_ps = acc[:, C + 2:C + 4, :]

        raw_in = [sem(f"raw_in{s}") for s in range(SLOTS)]
        act_done = sem("act_done")
        dve_done = sem("dve_done")
        used = sem("used")
        const_in = sem("const_in")
        ident0 = sem("ident0")
        const_ready = sem("const_ready")
        x_own_here = sem("x_own_here")
        x_ahead_here = sem("x_ahead_here")
        stats_ready = sem("stats_ready")
        pool_step = sem("pool_step")
        h_ready = sem("h_ready")
        tr_ready = sem("tr_ready")
        ht_ready = sem("ht_ready")
        g_ready = sem("g_ready")
        g_hi_kept = sem("g_hi_kept")
        g_kept = sem("g_kept")
        g_joined = sem("g_joined")
        G_hi_ready = sem("G_hi_ready")
        sums_free = sem("sums_free")
        total_ready = sem("total_ready")
        d_ready = sem("d_ready")
        stats_step = sem("stats_step")
        G_ready = sem("G_ready")
        base_ready = sem("base_ready")
        base_stored = sem("base_stored")
        base_step = sem("base_step")
        x_here_again = sem("x_here_again")
        base_here = sem("base_here")
        g_scaled = sem("g_scaled")
        full_base = sem("full_base")
        acc_free = sem("acc_free")
        scaled_ready = sem("scaled_ready")
        out_ready = sem("out_ready")
        out_stored = sem("out_stored")

        pool_gate = sem("pool_gate")
        dve_gate = sem("dve_gate")

        def made_ahead_before(ph):
            before = FIRST[ph.row0 - 1] if not ph.second and 0 < ph.row0 <= AHEAD else None
            assert before is None or before.ahead is not None
            return before

        def kept(ph):
            blocks = C * (OWN + ph.row0)
            for k in range(2):
                rows = slice(blocks + 2 * k, blocks + 2 * k + 2)
                yield G[:, rows, 0:F], g_ps[:, k, :].rearrange("p (c f) -> p c f", c=2), G[:, rows, SUMMED:SUMMED + F]

        def gate(eng, signal):
            eng.sem_inc(signal, 1)

        block = ctx.enter_context(nc.Block())

        @block.sync
        def _(sp):
            sp.dma_start(wt[:, :, :], w_t).then_inc(const_in, 16)
            sp.dma_start(bias_all[:, :], bias[0:1, :].broadcast_to([P, F])).then_inc(const_in, 16)

            def load(ph, row, loop, halves, t, n):
                for s, (what, unit, half) in enumerate(loop.kind):
                    sp.wait_ge(act_done, halves + s + 1)
                    sp.wait_ge(dve_done, halves + s + 1)
                    if what == "T":
                        src = adj_t[bass.ds(ph.at(row), 1), bass.ds(ph.t_first + t + unit, 1), half]
                    else:
                        src = adj_n[bass.ds(ph.at(row), 1), bass.ds(ph.row0 + n + unit, 1), half]
                    sp.dma_start(raw[loop.slot(s)][:, :, :], src.rearrange("a b p c j -> (a b p) c j")).then_inc(
                        raw_in[loop.slot(s)], 16)

            def row_block(ph, row):
                if ph.own is not None:
                    if ph.row0:
                        sp.wait_ge(h_ready, FIRST[ph.row0 - 1].own + 1)
                    sp.dma_start(x_own[:, :, :], x_rows[ph.row0]).then_inc(x_own_here, 16)
                for k in range(5):
                    if k == 2 and ph.ahead is not None:
                        if ph.row0:
                            sp.wait_ge(h_ready, FIRST[ph.row0 - 1].ahead + 1)
                        sp.dma_start(x_ahead[:, :, :], x_rows[OWN + ph.row0]).then_inc(x_ahead_here, 16)
                    for loop in ph.loop(k, row):
                        with sp.Fori(0, loop.count) as i:
                            load(ph, row, loop, loop.halves + len(loop.kind) * i,
                                 loop.t + units_of("T", loop.kind) * i, loop.n + units_of("N", loop.kind) * i)

            for ph in PHASES:
                with sp.Fori(0, ph.rows) as row:
                    row_block(ph, row)

        @block.gpsimd
        def _(pool):
            pool.memset(ident[:, :], 0.0).then_inc(ident0, 1)
            pool.memset(minus_half[:, :], -0.5)
            pool.memset(zeros[:, :].bitcast(f32), 0.0)
            pool.memset(G[:, :, F:F + 2].bitcast(f32), 1.0)
            pool.wait_ge(ident0, 1)
            pool.affine_select(out=ident[:, :], in_=ident[:, :], compare_op=ALU.not_equal, fill=1.0, base=0,
                               pattern=[[-1, P]], channel_multiplier=1).then_inc(const_ready, 1)
            pool.wait_ge(const_ready, 1)
            pool.wait_ge(const_in, 32)
            NORM_STEPS, D_STEPS = 6, 4

            def rsqrt(step, out, v):
                step(pool.tensor_tensor(out, v, minus_half[:, :], ALU.pow))
                step(pool.tensor_tensor(newton[:, :], out, out, ALU.mult))
                step(pool.tensor_tensor(newton[:, :], newton[:, :], v, ALU.mult))
                step(pool.tensor_scalar(newton[:, :], newton[:, :], -0.5, 1.5, ALU.mult, ALU.add))
                return pool.tensor_tensor(out, out, newton[:, :], ALU.mult)

            bias_c = bias_all[:, :].rearrange("p (a f) -> p a f", a=1).broadcast_to([P, C, F])

            def normalise(ph, step, ahead=False):
                x, number = (x_ahead, ph.ahead) if ahead else (x_own, ph.own)
                turn = int(ahead)
                pool.wait_ge(stats_ready, number + 1)
                gate(pool, pool_gate)
                step(pool.tensor_scalar(var_eps[:, :], meanvar[:, turn, :, 1], LN_EPS, None, ALU.add))
                step(rsqrt(step, rstd[:, :], var_eps[:, :]))
                if number:
                    pool.wait_ge(tr_ready, number)
                    gate(pool, pool_gate)
                for c in range(C):
                    last = pool.tensor_scalar(h[:, c, :], x[:, c, :], meanvar[:, turn, c, 0:1], rstd[:, c:c + 1],
                                              ALU.subtract, ALU.mult)
                last.then_inc(h_ready, 1)

            def steps_from(before):
                done = [before]

                def step(ins):
                    done[0] += 1
                    ins.then_inc(pool_step, 1)
                    pool.wait_ge(pool_step, done[0])
                    gate(pool, pool_gate)

                return step

            def first(ph, row, behind, row_behind):
                at = ph.at(row)
                if ph.ahead is not None:
                    normalise(ph, steps_from(NORM_STEPS * ph.ahead + D_STEPS * at), ahead=True)
                step = steps_from(NORM_STEPS * ph.normalised + D_STEPS * at)
                if ph.own is None:
                    pool.wait_ge(tr_ready, BLOCKS)
                    pool.wait_ge(g_kept, AHEAD)
                    pool.wait_ge(g_scaled, at)
                    gate(pool, pool_gate)
                    blocks = bass.ds(C * at, C)
                    pool.tensor_tensor(g_joint[:, :, :], G[:, blocks, 0:F].bitcast(f32),
                                       G[:, blocks, SUMMED:SUMMED + F].bitcast(f32), ALU.add).then_inc(g_joined, 1)
                pool.wait_ge(total_ready, at + 1)
                rsqrt(step, d_row[:, :], total[:, :]).then_inc(d_ready, 1)
                if behind.own is not None:
                    normalise(behind, step)
                pool.wait_ge(g_scaled, at + 1)
                gate(pool, pool_gate)
                if ph.t_units:
                    last = pool.tensor_tensor(base_out, g_all[:, :, :], part[:, :, 0:F], ALU.add)
                else:
                    last = pool.tensor_copy(base_out, g_all[:, :, :])
                last.then_inc(base_ready, 1)
                pool.wait_ge(base_ready, at + 1)
                gate(pool, pool_gate)
                pool.dma_start(base_dram[bass.ds(at, 1), :, :, :].rearrange("a p c f -> (a p) c f"),
                               base_out).then_inc(base_stored, 16)
                pool.wait_ge(base_stored, 16 * at + 16)
                if behind.second:
                    load_base(0)

            def load_base(at):
                pool.dma_start(base_in[:, :, :], base_dram[bass.ds(at, 1), :, :, :].rearrange(
                    "a p c f -> (a p) c f")).then_inc(base_here, 16)
                pool.dma_start(x_again[:, :, :], x_rows[bass.ds(at, 1), :, :, :].rearrange(
                    "a p c f -> (a p) c f")).then_inc(x_here_again, 16)

            def store_out(at):
                pool.dma_start(out_rows[bass.ds(at, 1), :, :, :].rearrange("a p c f -> (a p) c f"),
                               result[:, :, :]).then_inc(out_stored, 16)

            def second(ph, row, behind, row_behind):
                at = ph.at(row)
                pool.wait_ge(base_here, 16 * at + 16)
                gate(pool, pool_gate)
                d_wide = d_all[:, bass.ds(C * at, C)].rearrange("p (c a) -> p c a", a=1).broadcast_to([P, C, F])
                pool.tensor_tensor(base_in[:, :, :], base_in[:, :, :], d_wide, ALU.mult).then_inc(base_step, 1)
                pool.wait_ge(x_here_again, 16 * at + 16)
                pool.tensor_tensor(x_again[:, :, :], x_again[:, :, :], bias_c, ALU.add).then_inc(base_step, 1)
                pool.wait_ge(base_step, 2 * at + 2)
                pool.wait_ge(out_ready, at + 1)
                if ph is not SECOND[0] or row:
                    gate(pool, pool_gate)
                    store_out(at - 1)
                pool.tensor_tensor(base, base_in[:, :, :], x_again[:, :, :], ALU.add).then_inc(full_base, 1)
                if behind:
                    pool.wait_ge(full_base, at + 1)
                    gate(pool, pool_gate)
                    load_base(behind.at(row_behind))
                else:
                    pool.wait_ge(out_ready, at + 2)
                    gate(pool, pool_gate)
                    store_out(at)
                    pool.wait_ge(out_stored, 16 * BLOCKS)

            normalise(PHASES[0], steps_from(0))
            each_row(pool, PHASES, lambda ph, *rest: (second if ph.second else first)(ph, *rest))

        @block.scalar
        def _(act):
            act.sem_inc(act_done, SLOTS)

            def body(loop, halves, t, n):
                for s, (what, unit, half) in enumerate(loop.kind):
                    slot = raw[loop.slot(s)]
                    act.wait_ge(raw_in[loop.slot(s)], loop.came(halves, s))
                    if what == "T":
                        act.wait_ge(used, 2 * t + 2 * unit + half + 1)
                        nc.scalar.copy(a_hi[:, loop.split(unit, half)], slot[:, :, :]).then_inc(act_done, 1)
                    else:
                        nc.scalar.activation(slot[:, 0, :], slot[:, 0, :], ACT.Copy,
                                             accum_out=sums[:, HALF * half, bass.ds(n + unit, 1)]).then_inc(act_done, 1)

            def loops(ph, row, k):
                if k == 0 and not ph.second:
                    act.wait_ge(sums_free, ph.at(row) + 1)
                for loop in ph.loop(k, row):
                    with act.Fori(0, loop.count) as i:
                        body(loop, loop.halves + len(loop.kind) * i,
                             ph.t_before + ph.t_units * row + loop.t + units_of("T", loop.kind) * i,
                             loop.n + units_of("N", loop.kind) * i)

            def relu(number):
                act.wait_ge(tr_ready, number + 1)
                nc.scalar.activation(h_t[:, 0, :], tr_ps[:, 0, :], ACT.Relu)
                nc.scalar.activation(h_t[:, 1, :], tr_ps[:, 1, :], ACT.Relu).then_inc(ht_ready, 1)

            def step(ph, row, behind, row_behind):
                at = ph.at(row)
                before = made_ahead_before(ph)
                loops(ph, row, 2)
                if before:
                    act.wait_ge(g_ready, before.ahead + 1)
                    for hi, g, _ in kept(before):
                        last = nc.scalar.copy(hi, g)
                    last.then_inc(g_hi_kept, 1)
                loops(ph, row, 3)
                loops(ph, row, 4)
                if ph.own is not None:
                    relu(ph.own)
                if behind:
                    loops(behind, row_behind, 0)
                    loops(behind, row_behind, 1)
                if not ph.second:
                    act.wait_ge(d_ready, at + 1)
                    if ph.own is not None:
                        act.wait_ge(g_ready, ph.own + 1)
                    else:
                        act.wait_ge(g_joined, at - OWN + 1)
                    for c in range(C):
                        g = g_joint[:, c, :] if ph.own is None else g_ps[:, c // 2, F * (c % 2):F * (c % 2) + F]
                        last = nc.scalar.activation(g_all[:, c, :], g, ACT.Copy, scale=d_row[:, c:c + 1])
                    last.then_inc(g_scaled, 1)
                    if ph.ahead is not None:
                        relu(ph.ahead)
                else:
                    act.wait_ge(used, ph.halves_used(row))
                    act.wait_ge(out_ready, at + 1)
                    for c in range(C):
                        nc.scalar.activation(scaled[:, c, :], acc[:, bass.ds(C * ph.side(row) + c, 1), F:2 * F], ACT.Copy,
                                             scale=d_all[:, bass.ds(C * at + c, 1)]).then_inc(scaled_ready, 1)

            loops(PHASES[0], 0, 0)
            loops(PHASES[0], 0, 1)
            each_row(act, PHASES, step)

        @block.vector
        def _(dve):
            dve.sem_inc(dve_done, SLOTS)
            dve.sem_inc(acc_free, C)
            for buffer_free in (sums_free, out_ready):
                dve.sem_inc(buffer_free, 1)

            def body(loop, halves, n):
                for s, (what, unit, half) in enumerate(loop.kind):
                    slot = raw[loop.slot(s)]
                    if what == "T":
                        dve.wait_ge(act_done, SLOTS + halves + s + 1)
                        split = loop.split(unit, half)
                        nc.vector.tensor_tensor(a_lo[:, split], slot[:, :, :], a_hi[:, split].bitcast(f32),
                                                ALU.subtract).then_inc(dve_done, 1)
                    else:
                        dve.wait_ge(raw_in[loop.slot(s)], loop.came(halves, s))
                        nc.vector.tensor_reduce(sums[:, HALF * half + 1, bass.ds(n + unit, 1)], slot[:, 1, :], AX,
                                                ALU.add).then_inc(dve_done, 1)

            def loops(ph, row, k):
                for loop in ph.loop(k, row):
                    with dve.Fori(0, loop.count) as i:
                        body(loop, loop.halves + len(loop.kind) * i, loop.n + units_of("N", loop.kind) * i)

            def statistics(ph, ahead=False):
                x, number = (x_ahead, ph.ahead) if ahead else (x_own, ph.own)
                dve.wait_ge(x_ahead_here if ahead else x_own_here, 16 * ph.row0 + 16)
                for c in range(C):
                    last = nc.vector.bn_stats(stats[:, c, :], x[:, c, :])
                last.then_inc(stats_step, 1)
                dve.wait_ge(stats_step, number + 1)
                gate(dve, dve_gate)
                for c in range(C):
                    last = nc.vector.bn_aggr(meanvar[:, int(ahead), c, :], stats[:, c, :])
                last.then_inc(stats_ready, 1)

            def add_sums(ph, row):
                row_done = SLOTS + ph.halves_before + ph.halves * (row + 1)
                dve.wait_ge(act_done, row_done)
                dve.wait_ge(dve_done, row_done)
                nc.vector.tensor_reduce(total[:, :], sums[:, :, 0:ph.n_units], AX, ALU.add).then_inc(sums_free, 1)

            def empty_banks(ph, row):
                dve.wait_ge(sums_free, ph.at(row) + 2)
                if ph.t_units:
                    dve.wait_ge(base_stored, 16 * ph.at(row))
                    dve.wait_ge(used, ph.halves_used(row))
                    banks = acc[:, bass.ds(C * ph.side(row), C), 0:SUMMED]
                    for c in range(C):
                        nc.vector.tensor_copy(part[:, c, :], banks[:, c, :]).then_inc(acc_free, 1)
                    dve.wait_ge(acc_free, C * (ph.acc_before + row + 2))
                    nc.vector.scalar_tensor_tensor(out=total[:, :], in0=part[:, :, F], scalar=1.0, in1=total[:, :],
                                                   op0=ALU.add, op1=ALU.add).then_inc(total_ready, 1)
                else:
                    nc.vector.tensor_scalar(total[:, :], total[:, :], 1.0, None, ALU.add).then_inc(total_ready, 1)

            def finish_first(ph, row):
                at = ph.at(row)
                dve.wait_ge(d_ready, at + 1)
                nc.vector.tensor_copy(d_all[:, bass.ds(C * at, C)], d_row[:, :])
                dve.wait_ge(g_scaled, at + 1)
                nc.vector.tensor_copy(G[:, bass.ds(C * at, C), 0:F], g_all[:, :, :]).then_inc(G_hi_ready, 1)
                dve.wait_ge(G_hi_ready, at + 1)
                nc.vector.tensor_tensor(G[:, bass.ds(C * at, C), SUMMED:SUMMED + F], g_all[:, :, :],
                                        G[:, bass.ds(C * at, C), 0:F].bitcast(f32), ALU.subtract).then_inc(G_ready, 1)

            def finish_second(ph, row):
                at = ph.at(row)
                dve.wait_ge(full_base, at + 1)
                for c in range(C):
                    dve.wait_ge(scaled_ready, C * at + c + 1)
                    nc.vector.scalar_tensor_tensor(out=scaled[:, c, :], in0=acc[:, bass.ds(C * ph.side(row) + c, 1), 0:F],
                                                   scalar=d_all[:, bass.ds(C * at + c, 1)], in1=scaled[:, c, :],
                                                   op0=ALU.mult, op1=ALU.add).then_inc(acc_free, 1)
                dve.wait_ge(acc_free, C * (ph.acc_before + row + 2))
                if ph is not SECOND[0] or row:
                    dve.wait_ge(out_stored, 16 * at)
                nc.vector.tensor_tensor(result[:, :, :], scaled[:, :, :], base,
                                        ALU.add).then_inc(out_ready, 1)

            def step(ph, row, behind, row_behind):
                before = made_ahead_before(ph)
                loops(ph, row, 2)
                if before:
                    dve.wait_ge(g_hi_kept, before.row0 + 1)
                    for hi, g, lo in kept(before):
                        last = nc.vector.tensor_tensor(lo, g, hi.bitcast(f32), ALU.subtract)
                    last.then_inc(g_kept, 1)
                loops(ph, row, 3)
                if ph.ahead is not None:
                    statistics(ph, ahead=True)
                loops(ph, row, 4)
                if not ph.second:
                    add_sums(ph, row)
                    if behind.own is not None:
                        statistics(behind)
                if not ph.second and not behind.kept_busy:
                    empty_banks(ph, row)
                if behind:
                    loops(behind, row_behind, 0)
                if not ph.second and behind.kept_busy:
                    empty_banks(ph, row)
                if behind:
                    loops(behind, row_behind, 1)
                (finish_second if ph.second else finish_first)(ph, row)

            statistics(PHASES[0])
            loops(PHASES[0], 0, 0)
            loops(PHASES[0], 0, 1)
            each_row(dve, PHASES, step)

        @block.tensor
        def _(pe):
            pe.sem_inc(used, SLOTS)
            pe.wait_ge(const_ready, 1)
            pe.wait_ge(const_in, 32)

            def mm(out, stationary, moving, start=False):
                return nc.tensor.matmul(out, stationary, moving, start=start, stop=False, skip_group_check=True)

            def open_banks(bank, freed):
                for c in range(C):
                    pe.wait_ge(acc_free, freed + c + 1)
                    mm(acc[:, bank + c, 0:2], zeros[:, :], zeros[:, 0:2], start=True)

            def products(ph, loop, bank, halves, t):
                for s, (what, unit, half) in enumerate(loop.kind):
                    if what != "T":
                        continue
                    split = loop.split(unit, half)
                    for b in range(HALF):
                        Gb = G[:, bass.ds(C * (ph.t_first + t + unit) + HALF * half + b, 1), :]
                        both = Gb.rearrange("p a (two w) -> p (a two) w", two=2)[:, :, 0:F]
                        if b == 0:
                            pe.wait_ge(dve_done, SLOTS + halves + s + 1)
                        for c in range(C):
                            hi = a_hi[:, split, b, P * c:P * c + P]
                            lo = a_lo[:, split, b, P * c:P * c + P]
                            if ph.second:
                                mm(acc[:, bank + c, :], hi, both)
                                last = mm(acc[:, bank + c, 0:F], lo, Gb[:, :, 0:F])
                            else:
                                mm(acc[:, bank + c, 0:SUMMED], hi, Gb[:, :, 0:SUMMED])
                                mm(acc[:, bank + c, 0:F], hi, Gb[:, :, SUMMED:SUMMED + F])
                                last = mm(acc[:, bank + c, 0:SUMMED], lo, Gb[:, :, 0:SUMMED])
                    last.then_inc(used, 1)

            def loops(ph, row, k, bank):
                for loop in ph.loop(k, row):
                    t_units = units_of("T", loop.kind)
                    if t_units:
                        with pe.Fori(0, loop.count) as i:
                            products(ph, loop, bank, loop.halves + len(loop.kind) * i, loop.t + t_units * i)

            def transposes(number):
                pe.wait_ge(h_ready, number + 1)
                for k in range(2):
                    for c in range(C):
                        last = nc.tensor.transpose(tr_ps[:, k, P * c:P * c + P], h[:, c, P * k:P * k + P], ident[:, :])
                last.then_inc(tr_ready, 1)

            def make_g(number):
                pe.wait_ge(ht_ready, number + 1)
                for c in range(C):
                    for k in range(2):
                        last = nc.tensor.matmul(g_ps[:, c // 2, F * (c % 2):F * (c % 2) + F],
                                                h_t[:, k, P * c:P * c + P], wt[:, k, :],
                                                start=(k == 0), stop=(k == 1))
                last.then_inc(g_ready, 1)

            def first(ph, row, bank):
                before = made_ahead_before(ph)
                if ph.t_units:
                    open_banks(bank, C * (ph.acc_before + row - (1 if ph.alternate else 0)))
                loops(ph, row, 0, bank)
                loops(ph, row, 1, bank)
                if before:
                    pe.wait_ge(g_scaled, before.row0 + 1)
                    make_g(before.ahead)
                if ph.own is not None:
                    transposes(ph.own)
                if ph.row0:
                    pe.wait_ge(G_ready, ph.row0)
                loops(ph, row, 2, bank)
                loops(ph, row, 3, bank)
                loops(ph, row, 4, bank)
                if ph.own is not None:
                    if before:
                        pe.wait_ge(g_kept, ph.row0)
                    elif ph.row0:
                        pe.wait_ge(g_scaled, ph.row0)
                    make_g(ph.own)
                if ph.ahead is not None:
                    transposes(ph.ahead)

            def second(ph, row, bank):
                open_banks(bank, C * (ph.acc_before + row - 1))
                loops(ph, row, 0, bank)
                loops(ph, row, 1, bank)
                pe.wait_ge(G_ready, BLOCKS)
                loops(ph, row, 2, bank)
                loops(ph, row, 3, bank)
                loops(ph, row, 4, bank)

            for ph in PHASES:
                if not ph.second and ph.row0 > 1:
                    pe.wait_ge(G_ready, ph.row0 - 1)
                with pe.Fori(0, (ph.rows + 1) // 2) as pair:
                    for k in range(min(ph.rows, 2)):
                        row = 2 * pair + k if ph.rows > 1 else 0
                        if ph.second:
                            second(ph, row, C * ph.side(k))
                        else:
                            first(ph, row, C * ph.side(k))


def kernel(x, adj, L0_gnn_W, L0_gnn_b):
    import numpy as np
    import concourse.bacc as bacc
    from concourse.bass_utils import run_bass_kernel_spmd

    x, adj = np.asarray(x), np.asarray(adj)
    W, b = np.asarray(L0_gnn_W), np.asarray(L0_gnn_b)
    x_rows = np.ascontiguousarray(x.reshape(BLOCKS, C, P, F).transpose(0, 2, 1, 3))
    adj_t = np.ascontiguousarray(adj.reshape(BLOCKS, R, BLOCKS, 2, HALF, P).transpose(0, 2, 3, 5, 4, 1))
    adj_n = np.ascontiguousarray(adj.reshape(BLOCKS, 2, HALF, P, BLOCKS, R).transpose(0, 4, 1, 3, 2, 5))
    w_t = np.ascontiguousarray(W.T.reshape(2, P, F).transpose(1, 0, 2))
    bias = np.ascontiguousarray(b.reshape(1, F))
    given = {"x_rows": x_rows, "adj_t": adj_t, "adj_n": adj_n, "w_t": w_t, "bias": bias}

    nc = bacc.Bacc("TRN2", target_bir_lowering=False, num_devices=1)
    args = [nc.dram_tensor(name, a.shape, mybir.dt.from_np(a.dtype), kind="ExternalInput").ap()
            for name, a in given.items()]
    out = nc.dram_tensor("out_rows", x_rows.shape, mybir.dt.float32, kind="ExternalOutput").ap()
    gnn_kernel(nc, *args, out)
    r = run_bass_kernel_spmd(nc, [given], core_ids=[0])
    got = r.results[0]["out_rows"]
    return np.ascontiguousarray(got.transpose(0, 2, 1, 3).reshape(N, F))
```
